# Optimizing a Trainium2 kernel written in Bass

```python
import numpy as np
import jax
import jax.numpy as jnp

def _softmax(x, axis=-1):
    return jax.nn.softmax(x, axis=axis)

def _gelu(x):
    return jax.nn.gelu(x, approximate=True)

def _silu(x):
    return jax.nn.silu(x)

def _sigmoid(x):
    return jax.nn.sigmoid(x)

def _layernorm(x, axis=-1, eps=1e-05):
    m = jnp.mean(x, axis=axis, keepdims=True)
    v = jnp.var(x, axis=axis, keepdims=True)
    return (x - m) / jnp.sqrt(v + eps)

def _scatter_add(tgt, idx, src, axis=0):
    return tgt.at[idx].add(src)

def _segment_sum(src, seg, n):
    return jax.ops.segment_sum(src, seg, n)
kernel_name = 'mk_adj_resnorm_d1_adj_r2_6f2131'

def setup_inputs(seed: int=0):
    np.random.seed(seed)
    _w = jnp.asarray

    def _rec_inputs():
        import jax
        import jax.numpy as jnp
        _gk = jax.random.key(seed)
        x = 0.5 + 0.2887 * jax.random.normal(jax.random.fold_in(_gk, 1), (4096, 256), jnp.float32)
        _a = jax.random.bernoulli(jax.random.fold_in(_gk, 2), 0.00195312, (4096, 4096))
        _a = jnp.logical_or(_a, jnp.eye(4096, dtype=bool))
        _af = _a.astype(jnp.float32)
        _af = _af * jax.random.uniform(jax.random.fold_in(_gk, 3), (4096, 4096), jnp.float32, 0.05, 1)
        adj = _af
        return (x, adj)
    x, adj = _rec_inputs()

    def _L0_gnn_setup():
        import jax, jax.numpy as jnp
        import numpy as np
        N = 4096
        IN_C = 256
        OUT_C = 256
        key = jax.random.key(seed)
        k1, k2, k3 = jax.random.split(key, 3)
        adj_matrix = jax.random.uniform(k1, (N, N), dtype=jnp.float32)
        x = jax.random.uniform(k2, (N, IN_C), dtype=jnp.float32)
        weight = jax.random.uniform(k3, (IN_C, OUT_C), dtype=jnp.float32) / 4 - 0.125
        return {'x': x, 'adj_matrix': adj_matrix, 'weight': weight}
    _L0_gnn_all = _L0_gnn_setup()
    _L0_gnn_in = {k: v for k, v in _L0_gnn_all.items() if k in ('weight',)}
    del _L0_gnn_all
    return {'x': x, 'adj': adj, 'L0_gnn_weight': _L0_gnn_in['weight']}

def reference(x, adj, L0_gnn_weight):
    import jax
    import jax.numpy as jnp

    def _L0_gnn_ref(x, adj_matrix, weight):
        import jax, jax.numpy as jnp
        import numpy as np
        N = 4096
        IN_C = 256
        OUT_C = 256
        n = adj_matrix.shape[0]
        deg = jnp.sum(adj_matrix, axis=1)
        dinv = (deg + 1.0) ** (-0.5)
        aug = dinv[:, None] * (adj_matrix + jnp.eye(n, dtype=adj_matrix.dtype)) * dinv[None, :]
        return jax.nn.relu(aug @ x @ weight)
    x = _layernorm(x + _L0_gnn_ref(x, adj, L0_gnn_weight), axis=-1)
    return x

_drawn_inputs = setup_inputs


def setup_inputs(seed=0):
    import zlib

    import numpy as np

    out = dict(_drawn_inputs(seed))
    spreads = {}
    factors = {}
    for name, (base, spread) in spreads.items():
        noise = np.random.default_rng([zlib.crc32(name.encode()), seed]).standard_normal(out[name].shape)
        drawn = base * np.exp(spread * noise) if base else spread * noise
        out[name] = jnp.asarray(drawn.astype(out[name].dtype))
    for name, factor in factors.items():
        out[name] = (out[name] * factor).astype(out[name].dtype)
    return out
```

```python
import concourse.bass as bass
from concourse import mybir
from contextlib import ExitStack

P = 128
N = 4096
C = 256
R = 512
T = R // P
B = N // R
BLK = T * R
HALF = BLK // 2
EPS = 1e-5

RAW_SLOTS = 4
SPLIT_SLOTS = 2
NAT_SLOTS = 2
XT_SLOTS = 2
X_SLOTS = 4


def tri(k):
    return k * (k + 1) // 2


PHASE1 = tri(B)
TOTAL = B * B


def upper(k):
    return sum(B - 1 - r for r in range(k))


def schedule():
    rows = [(k, tri(k), 0, k + 1) for k in range(B)]
    rows += [(k, PHASE1 + upper(k), k + 1, B - 1 - k) for k in range(B - 1)]
    return rows


def nat_turns(k):
    left, slots = B - 1 - k, max(1, k - 1)
    turns = [left // slots + (i < left % slots) for i in range(slots)]
    return turns + [0] * (k + 1 - slots)


def build(nc, at, nat, xt, w, x, out):
    f32 = mybir.dt.float32
    f32r = mybir.dt.float32r
    ALU = mybir.AluOpType
    ACT = mybir.ActivationFunctionType
    AX = mybir.AxisListType

    ctx = ExitStack()
    with ctx:
        def sb(name, shape, dt=f32):
            return ctx.enter_context(nc.sbuf_tensor(name, shape, dt))

        def bank(name):
            return ctx.enter_context(nc.psum_tensor(name, [P, 512], f32))

        def sem(name):
            return ctx.enter_context(nc.semaphore(name))

        raw = sb("raw", [P, RAW_SLOTS * BLK])
        hi = sb("hi", [P, SPLIT_SLOTS * BLK], f32r)
        lo = sb("lo", [P, SPLIT_SLOTS * BLK], f32r)
        hi_f = hi[:, :].bitcast(f32)
        natx = sb("natx", [P, NAT_SLOTS * BLK])
        y = sb("y", [P, N // P, 2 * C], f32r)
        y_f = y[:, :, :].bitcast(f32)
        acc = sb("acc", [P, N // P, C])
        colsum = sb("colsum", [P, BLK])
        folded = sb("folded", [P, R])
        xts = sb("xts", [P, XT_SLOTS, 2, R])
        ws = sb("ws", [P, 2, C])
        ones = sb("ones", [P, 1])
        natsum = sb("natsum", [P, B, T, B])
        natdeg = sb("natdeg", [P, T])
        deg = sb("deg", [P, T])
        root = sb("root", [P, T])
        inv = sb("inv", [P, T])
        tmp = sb("tmp", [P, T])
        dinv = sb("dinv", [P, N // P])
        stats = sb("stats", [P, T, 6])
        moments = sb("moments", [P, T, 2])
        var = sb("var", [P, T])
        rstd = sb("rstd", [P, T])

        banks = [bank(f"sum{t}") for t in range(T)]
        xw_banks = [bank(f"xw{h}") for h in range(2)]
        deg_bank = bank("degsum")

        w_loaded = sem("w_loaded")
        xt_loaded = [sem(f"xt_loaded{s}") for s in range(XT_SLOTS)]
        raw_loaded = [sem(f"raw_loaded{s}") for s in range(RAW_SLOTS)]
        nat_loaded = [sem(f"nat_loaded{s}") for s in range(NAT_SLOTS)]
        x_loaded = [sem(f"x_loaded{s}") for s in range(X_SLOTS)]
        stored = [sem(f"stored{s}") for s in range(X_SLOTS)]
        raw_ready = sem("raw_ready")
        consts = sem("consts")
        xw_done = sem("xw_done")
        xw_copied = sem("xw_copied")
        hi_ready = sem("hi_ready")
        lo_ready = sem("lo_ready")
        tiles_done = sem("tiles_done")
        bank_free = sem("bank_free")
        summed = sem("summed")
        fold_done = sem("fold_done")
        nat_summed = sem("nat_summed")
        deg_summed = sem("deg_summed")
        deg_ready = sem("deg_ready")
        root_ready = sem("root_ready")
        dinv_ready = sem("dinv_ready")
        scaled = sem("scaled")
        yhi_ready = sem("yhi_ready")
        y_ready = sem("y_ready")
        relu_done = sem("relu_done")
        normed = sem("normed")
        step = sem("step")

        DIAG = [tri(k) + k for k in range(B)]
        ROWS = schedule()
        FINISH = [B - 1] + list(range(B - 1))

        def raw_at(n, a=0, size=BLK):
            return raw[:, bass.ds((n % RAW_SLOTS) * BLK + a, size)]

        def split_at(tensor, n, a=0, size=BLK):
            return tensor[:, bass.ds((n % SPLIT_SLOTS) * BLK + a, size)]

        def xslot(e):
            s = e % X_SLOTS
            return natx[:, s * T * C:(s + 1) * T * C].rearrange("p (t c) -> p t c", c=C)

        def sweep(eng, start, stop, body):
            if stop - start >= 3:
                with eng.Fori(start, stop) as i:
                    body(i)
            else:
                for i in range(start, stop):
                    body(i)

        block = ctx.enter_context(nc.Block())

        @block.sync
        def _(sp):
            sp.dma_start(ws[:, :, :], w).then_inc(w_loaded, 16)

            def load_xt(b):
                if b >= XT_SLOTS:
                    sp.wait_ge(xw_done, 2 * (b - XT_SLOTS) + 2)
                sp.dma_start(xts[:, b % XT_SLOTS, :, :], xt[b]).then_inc(xt_loaded[b % XT_SLOTS], 16)

            def load_raw(n):
                if n >= RAW_SLOTS:
                    sp.wait_ge(lo_ready, 2 * (n - RAW_SLOTS) + 2)
                sp.dma_start(raw_at(n), at[n]).then_inc(raw_loaded[n % RAW_SLOTS], 16)

            def load_nat(m):
                if m >= NAT_SLOTS:
                    sp.wait_ge(nat_summed, m - NAT_SLOTS + 1)
                s = m % NAT_SLOTS
                sp.dma_start(natx[:, s * BLK:(s + 1) * BLK], nat[m]).then_inc(nat_loaded[s], 16)

            m = 0
            b = 0
            for k in range(B):
                if k < 3:
                    while b < (2, 4, 6)[k]:
                        load_xt(b)
                        b += 1
                    for j in range(k + 1):
                        load_raw(tri(k) + j)
                    for i in range(B - 1 - k):
                        load_nat(m)
                        m += 1
                        if i in (1, 3) and b < (4, 6, 8)[k]:
                            load_xt(b)
                            b += 1
                else:
                    turns = nat_turns(k)
                    for j in range(k + 1):
                        load_raw(tri(k) + j)
                        for _ in range(turns[j]):
                            load_nat(m)
                            m += 1

            sp.wait_ge(nat_summed, upper(B))

            def load_x(e):
                if e >= X_SLOTS:
                    sp.wait_ge(stored[e % X_SLOTS], 16 * (e // X_SLOTS))
                sp.dma_start(xslot(e), x[FINISH[e]]).then_inc(x_loaded[e % X_SLOTS], 16)

            def store(e):
                sp.wait_ge(normed, T * (e + 1))
                sp.dma_start(out[FINISH[e]], xslot(e)).then_inc(stored[e % X_SLOTS], 16)

            for e in range(X_SLOTS):
                load_x(e)
            last = {e: ROWS[B - 1 + e][1] + ROWS[B - 1 + e][3] - 1 for e in range(B)}
            for n in range(PHASE1, TOTAL):
                load_raw(n)
                for e in range(B):
                    if n == last[e] + RAW_SLOTS + 4:
                        store(e)
                        if e + X_SLOTS < B:
                            load_x(e + X_SLOTS)
            for e in range(B):
                if last[e] + RAW_SLOTS + 4 >= TOTAL:
                    store(e)
                    if e + X_SLOTS < B:
                        load_x(e + X_SLOTS)
            for s in range(X_SLOTS):
                sp.wait_ge(stored[s], 16 * len(range(s, B, X_SLOTS)))

        @block.gpsimd
        def _(pool):
            with pool.Fori(0, TOTAL // RAW_SLOTS) as i:
                for s in range(RAW_SLOTS):
                    pool.wait_ge(raw_loaded[s], 16 * (i + 1))
                    pool.sem_inc(raw_ready, 1)

        @block.scalar
        def _(act):
            def round_hi(n):
                act.wait_ge(raw_ready, n + 1)
                if not isinstance(n, int) or n >= SPLIT_SLOTS:
                    act.wait_ge(tiles_done, T * (n - SPLIT_SLOTS + 1))
                for h in range(2):
                    nc.scalar.activation(split_at(hi, n, h * HALF, HALF), raw_at(n, h * HALF, HALF),
                                         ACT.Copy).then_inc(hi_ready, 1)

            def sum_nat(m, k, i):
                s = m % NAT_SLOTS
                act.wait_ge(nat_loaded[s], 16 * (m // NAT_SLOTS + 1))
                if m == 0:
                    act.wait_ge(consts, 1)
                for t in range(T):
                    a = natx[:, s * BLK + t * R:s * BLK + (t + 1) * R]
                    last = nc.scalar.activation(a, a, ACT.Copy, accum_out=natsum[:, k, t, i:i + 1])
                last.then_inc(nat_summed, 1)

            def copy_xw(b):
                for h in range(2):
                    act.wait_ge(xw_done, 2 * b + h + 1)
                    nc.scalar.activation(acc[:, b * T + 2 * h:b * T + 2 * h + 2, :], xw_banks[h][:, :],
                                         ACT.Copy).then_inc(xw_copied, 1)

            def scale_y(k):
                act.wait_ge(deg_ready, k + 1)
                nc.scalar.activation(root[:, :], deg[:, :], ACT.Sqrt).then_inc(root_ready, 1)
                act.wait_ge(dinv_ready, k + 1)
                for t in range(T):
                    a = acc[:, k * T + t, :]
                    nc.scalar.activation(a, a, ACT.Copy, scale=dinv[:, k * T + t:k * T + t + 1]).then_inc(scaled, 1)
                act.wait_ge(scaled, T * (k + 1))
                nc.scalar.activation(y[:, k * T:(k + 1) * T, 0:C], acc[:, k * T:(k + 1) * T, :],
                                     ACT.Copy).then_inc(yhi_ready, 1)

            def relu(e):
                k = FINISH[e]
                for t in range(T):
                    act.wait_ge(bank_free, T * (B - 1 + e) + t + 1)
                    a = acc[:, k * T + t, :]
                    nc.scalar.activation(a, a, ACT.Relu, scale=dinv[:, k * T + t:k * T + t + 1]).then_inc(relu_done, 1)

            def norm_root(e):
                act.wait_ge(deg_ready, B + e + 1)
                nc.scalar.activation(root[:, :], var[:, :], ACT.Sqrt).then_inc(root_ready, 1)

            m = 0
            for k in range(B):
                if k < 3:
                    sweep(act, tri(k), tri(k) + max(k, 1), round_hi)
                    b = 2 * k
                    for i in range(B - 1 - k):
                        if i == 0 and k == 0:
                            copy_xw(0)
                            copy_xw(1)
                        sum_nat(m, k, i)
                        m += 1
                        if i in (2, 4):
                            copy_xw(2 * k + 2 + (i == 4))
                    if k:
                        round_hi(DIAG[k])
                    scale_y(k)
                else:
                    turns = nat_turns(k)
                    i = 0
                    busy = sum(1 for v in turns if v)
                    for j in range(busy):
                        round_hi(tri(k) + j)
                        for _ in range(turns[j]):
                            sum_nat(m, k, i)
                            m += 1
                            i += 1
                    sweep(act, tri(k) + busy, tri(k) + k + 1, round_hi)
                    scale_y(k)

            for e in range(B):
                if e + 1 < B:
                    _, n0, _, count = ROWS[B + e]
                    round_hi(n0)
                    relu(e)
                    if count > 1:
                        round_hi(n0 + 1)
                    norm_root(e)
                    sweep(act, n0 + 2, n0 + count, round_hi)
                else:
                    relu(e)
                    norm_root(e)

        @block.vector
        def _(dve):
            chain = [0]

            def link(instruction):
                chain[0] += 1
                instruction.then_inc(step, 1)
                dve.wait_ge(step, chain[0])

            nc.vector.memset(ones[:, :], 1.0)
            nc.vector.memset(natsum[:, :, :, :], 0.0).then_inc(consts, 1)

            sums = [0]

            def first_sum(k):
                n = tri(k)
                if k == 0:
                    dve.wait_ge(raw_ready, 1)
                    return
                dve.wait_ge(raw_ready, n + 2)
                nc.vector.tensor_tensor(colsum[:, :], raw_at(n), raw_at(n + 1), ALU.add).then_inc(summed, 1)
                sums[0] += 1

            def add_sum(n, base):
                dve.wait_ge(raw_ready, n + 1)
                dve.wait_ge(summed, n - base)
                nc.vector.tensor_tensor(colsum[:, :], colsum[:, :], raw_at(n), ALU.add).then_inc(summed, 1)

            def fold(k):
                src = raw_at(0) if k == 0 else colsum[:, :]
                if k:
                    dve.wait_ge(summed, sums[0])
                link(nc.vector.tensor_tensor(colsum[:, 0:HALF], src[:, 0:HALF], src[:, HALF:BLK], ALU.add))
                if k:
                    dve.wait_ge(deg_summed, k)
                nc.vector.tensor_tensor(folded[:, :], colsum[:, 0:R], colsum[:, R:2 * R],
                                        ALU.add).then_inc(fold_done, 1)

            def take_lo(n):
                for h in range(2):
                    dve.wait_ge(hi_ready, 2 * n + h + 1)
                    nc.vector.tensor_tensor(split_at(lo, n, h * HALF, HALF), raw_at(n, h * HALF, HALF),
                                            split_at(hi_f, n, h * HALF, HALF), ALU.subtract).then_inc(lo_ready, 1)

            def refine(d, result):
                link(nc.vector.reciprocal(inv[:, :], root[:, :]))
                link(nc.vector.scalar_tensor_tensor(out=tmp[:, :], in0=inv[:, :], scalar=-0.5, in1=inv[:, :],
                                                    op0=ALU.mult, op1=ALU.mult))
                link(nc.vector.tensor_tensor(tmp[:, :], tmp[:, :], d, ALU.mult))
                return nc.vector.scalar_tensor_tensor(out=result, in0=tmp[:, :], scalar=1.5, in1=inv[:, :],
                                                      op0=ALU.add, op1=ALU.mult)

            def scale_factors(k):
                dve.wait_ge(nat_summed, upper(k + 1))
                link(nc.vector.tensor_reduce(natdeg[:, :], natsum[:, k, :, :], AX.X, ALU.add))
                dve.wait_ge(deg_summed, k + 1)
                nc.vector.scalar_tensor_tensor(out=deg[:, :], in0=deg_bank[:, 0:T], scalar=1.0, in1=natdeg[:, :],
                                               op0=ALU.add, op1=ALU.add).then_inc(deg_ready, 1)
                dve.wait_ge(root_ready, k + 1)
                dve.wait_ge(deg_ready, k + 1)
                refine(deg[:, :], dinv[:, k * T:(k + 1) * T]).then_inc(dinv_ready, 1)

            def lo_of_y(k):
                dve.wait_ge(yhi_ready, k + 1)
                nc.vector.tensor_tensor(y[:, k * T:(k + 1) * T, C:2 * C], acc[:, k * T:(k + 1) * T, :],
                                        y_f[:, k * T:(k + 1) * T, 0:C], ALU.subtract).then_inc(y_ready, 1)

            def read_banks(g):
                k, n0, _, count = ROWS[g]
                for t in range(T):
                    a = acc[:, k * T + t, :]
                    dve.wait_ge(tiles_done, T * (n0 + count - 1) + t + 1)
                    link(nc.vector.tensor_tensor(a, a, banks[t][:, 0:C], ALU.add))
                    nc.vector.tensor_tensor(a, a, banks[t][:, C:2 * C], ALU.add).then_inc(bank_free, 1)

            def residual(e):
                k = FINISH[e]
                xe = xslot(e)
                dve.wait_ge(x_loaded[e % X_SLOTS], 16 * (e // X_SLOTS + 1))
                for t in range(T):
                    dve.wait_ge(relu_done, T * e + t + 1)
                    link(nc.vector.tensor_tensor(xe[:, t, :], xe[:, t, :], acc[:, k * T + t, :], ALU.add))
                    link(nc.vector.bn_stats(stats[:, t, :], xe[:, t, :]))
                    last = nc.vector.bn_aggr(moments[:, t, :], stats[:, t, :])
                link(last)
                nc.vector.tensor_scalar(var[:, :], moments[:, :, 1], EPS, None, ALU.add).then_inc(deg_ready, 1)

            def normalise(e):
                xe = xslot(e)
                dve.wait_ge(root_ready, B + e + 1)
                dve.wait_ge(deg_ready, B + e + 1)
                link(refine(var[:, :], rstd[:, :]))
                for t in range(T):
                    nc.vector.tensor_scalar(xe[:, t, :], xe[:, t, :], moments[:, t, 0:1], rstd[:, t:t + 1],
                                            ALU.subtract, ALU.mult).then_inc(normed, 1)

            for k in range(B):
                n0 = tri(k)
                first_sum(k)
                base = n0 + 2 - sums[0]

                def chained(n):
                    add_sum(n, base)

                if k >= 2:
                    chained(n0 + 2)
                    sums[0] += 1
                if k <= 2:
                    fold(k)
                take_lo(n0)
                if k:
                    read_banks(k - 1)

                def middle(i):
                    chained(i + 2)
                    take_lo(i)

                if k >= 3:
                    sweep(dve, n0 + 1, n0 + k - 1, middle)
                    sums[0] += k - 2
                    fold(k)
                    take_lo(n0 + k - 1)
                elif k == 2:
                    take_lo(n0 + 1)
                if k:
                    scale_factors(k)
                    take_lo(n0 + k)
                else:
                    scale_factors(k)
                lo_of_y(k)

            for e in range(B):
                if e + 1 < B:
                    _, n0, _, count = ROWS[B + e]
                    take_lo(n0)
                    read_banks(B - 1 + e)
                    if count > 1:
                        take_lo(n0 + 1)
                    residual(e)
                    if count > 2:
                        take_lo(n0 + 2)
                    normalise(e)
                    sweep(dve, n0 + 3, n0 + count, take_lo)
                else:
                    read_banks(B - 1 + e)
                    residual(e)
                    normalise(e)

        @block.tensor
        def _(pe):
            def xw(b):
                s = b % XT_SLOTS
                if b == 0:
                    pe.wait_ge(w_loaded, 16)
                pe.wait_ge(xt_loaded[s], 16 * (b // XT_SLOTS + 1))
                for h in range(2):
                    if b:
                        pe.wait_ge(xw_copied, 2 * (b - 1) + h + 1)
                    for q in range(2):
                        t = 2 * h + q
                        for c in range(2):
                            last = nc.tensor.matmul(xw_banks[h][:, q * C:(q + 1) * C],
                                                    xts[:, s, c, t * P:(t + 1) * P], ws[:, c, :],
                                                    start=(c == 0), stop=(c == 1))
                    last.then_inc(xw_done, 1)

            def sum_degrees(k):
                pe.wait_ge(fold_done, k + 1)
                if k == 0:
                    pe.wait_ge(consts, 1)
                else:
                    pe.wait_ge(deg_ready, k)
                for t in range(T):
                    last = nc.tensor.matmul(deg_bank[:, t:t + 1], folded[:, t * P:(t + 1) * P], ones[:, :],
                                            start=True, stop=True)
                last.then_inc(deg_summed, 1)

            def multiply(g, n, j, s, first, last):
                pe.wait_ge(lo_ready, 2 * n + 2)
                pe.wait_ge(y_ready, j + 1)
                for t in range(T):
                    if first and g:
                        pe.wait_ge(bank_free, T * (g - 1) + t + 1)
                    for u in range(T):
                        a = s * BLK + u * R + t * P
                        row = j * T + u
                        opens, closes = first and u == 0, last and u == T - 1

                        def by_hi():
                            return nc.tensor.matmul(banks[t][:, :], hi[:, a:a + P], y[:, row, :],
                                                    start=opens, stop=closes)

                        def by_lo():
                            return nc.tensor.matmul(banks[t][:, 0:C], lo[:, a:a + P], y[:, row, 0:C],
                                                    start=False, stop=False)

                        if opens:
                            by_hi()
                            done = by_lo()
                        else:
                            by_lo()
                            done = by_hi()
                    done.then_inc(tiles_done, 1)

            def row_group(g, before):
                k, n0, j0, count = ROWS[g]

                def one(i, s):
                    multiply(g, n0 + i, j0 + i, s, isinstance(i, int) and i == 0,
                             isinstance(i, int) and i == count - 1)

                i = 0
                while i < count:
                    for extra in before.get(i, ()):
                        extra()
                    stop = min([count - 1] + [b for b in before if b > i])
                    pairs = (stop - i) // 2
                    if i and pairs >= 2:
                        with pe.Fori(0, pairs) as q:
                            for h in range(2):
                                one(q * 2 + (i + h), (n0 + i + h) % SPLIT_SLOTS)
                        i += 2 * pairs
                    else:
                        one(i, (n0 + i) % SPLIT_SLOTS)
                        i += 1

            for b in range(4):
                xw(b)
            row_group(0, {0: [lambda: sum_degrees(0)]})
            row_group(1, {1: [lambda: xw(4), lambda: xw(5), lambda: sum_degrees(1)]})
            row_group(2, {2: [lambda: xw(6), lambda: xw(7), lambda: sum_degrees(2)]})
            for k in range(3, B):
                row_group(k, {k - 1: [lambda: sum_degrees(k)]})
            for g in range(B, 2 * B - 1):
                row_group(g, {})


def kernel(x, adj, L0_gnn_weight):
    import numpy as np
    import concourse.bacc as bacc
    from concourse.bass_utils import run_bass_kernel_spmd

    x, adj, weight = (np.asarray(a) for a in (x, adj, L0_gnn_weight))
    blocks = adj.reshape(B, T, P, B, T, P)
    lower = [(k, j) for k in range(B) for j in range(k + 1)]
    higher = [(k, j) for k in range(B) for j in range(k + 1, B)]
    at = np.stack([blocks[k, :, :, j].transpose(3, 2, 0, 1).reshape(P, BLK) for k, j in lower + higher])
    nat = np.stack([blocks[k, :, :, j].transpose(1, 0, 2, 3).reshape(P, BLK) for k, j in higher])
    xt = np.ascontiguousarray(x.reshape(B, R, 2, P).transpose(0, 3, 2, 1))
    xn = np.ascontiguousarray(x.reshape(B, T, P, C).transpose(0, 2, 1, 3))
    wn = np.ascontiguousarray(weight.reshape(2, P, C).transpose(1, 0, 2))

    nc = bacc.Bacc("TRN2", target_bir_lowering=False, num_devices=1)
    arrays = {"in_at": at, "in_nat": nat, "in_xt": xt, "in_w": wn, "in_x": xn}
    aps = [nc.dram_tensor(name, a.shape, mybir.dt.from_np(a.dtype), kind="ExternalInput").ap()
           for name, a in arrays.items()]
    aps.append(nc.dram_tensor("out", xn.shape, mybir.dt.float32, kind="ExternalOutput").ap())
    build(nc, *aps)
    r = run_bass_kernel_spmd(nc, [arrays], core_ids=[0])
    got = r.results[0]["out"]
    return np.ascontiguousarray(got.transpose(0, 2, 1, 3)).reshape(N, C)
```

```python
import concourse.bass as bass
from concourse import mybir
from contextlib import ExitStack

P = 128
N = 4096
C = 256
CT = C // P
R = 512
T = R // P
B = N // R
BLK = T * R
HALF = BLK // 2
EPS = 1e-5

RAW_SLOTS = 4
SPLIT_SLOTS = 2
NAT_SLOTS = 2
XT_SLOTS = 2
X_SLOTS = 4
EARLY = 3


def tri(k):
    return k * (k + 1) // 2


PHASE1 = tri(B)
TOTAL = B * B


def upper(k):
    return sum(B - 1 - r for r in range(k))


def schedule():
    rows = [(k, tri(k), 0, k + 1) for k in range(B)]
    rows += [(k, PHASE1 + upper(k), k + 1, B - 1 - k) for k in range(B - 1)]
    return rows


def nat_turns(k):
    left, slots = B - 1 - k, k - 1
    turns = [left // slots + (i < left % slots) for i in range(slots)]
    return turns + [0] * (k + 1 - slots)


def build(nc, at, nat, xt, w, x, out):
    f32 = mybir.dt.float32
    f32r = mybir.dt.float32r
    ALU = mybir.AluOpType
    ACT = mybir.ActivationFunctionType
    AX = mybir.AxisListType

    ctx = ExitStack()
    with ctx:
        def sb(name, shape, dt=f32):
            return ctx.enter_context(nc.sbuf_tensor(name, shape, dt))

        def bank(name):
            return ctx.enter_context(nc.psum_tensor(name, [P, 512], f32))

        def sem(name):
            return ctx.enter_context(nc.semaphore(name))

        raw = sb("raw", [P, RAW_SLOTS * BLK + R])
        hi = sb("hi", [P, SPLIT_SLOTS * BLK], f32r)
        lo = sb("lo", [P, SPLIT_SLOTS * BLK], f32r)
        hi_f = hi[:, :].bitcast(f32)
        natx = sb("natx", [P, NAT_SLOTS * BLK])
        y = sb("y", [P, N // P, 2, C], f32r)
        y_f = y[:, :, :, :].bitcast(f32)
        xw = sb("xw", [P, N // P, C])
        colsum = sb("colsum", [P, BLK])
        folded = sb("folded", [P, R])
        xts = sb("xts", [P, XT_SLOTS, CT, R])
        ws = sb("ws", [P, CT, C])
        ones = sb("ones", [P, 1])
        ident = sb("ident", [P, P])
        natsum = sb("natsum", [P, B, T, B])
        natdeg = sb("natdeg", [P, T])
        deg = sb("deg", [P, T])
        root = sb("root", [P, T])
        inv = sb("inv", [P, T])
        tmp = sb("tmp", [P, T])
        dinv = sb("dinv", [P, N // P])
        stats = sb("stats", [P, T, 6])
        moments = sb("moments", [P, T, 2])
        var = sb("var", [P, T])
        rstd = sb("rstd", [P, T])

        zbanks = [[bank(f"z{s}{c}") for c in range(CT)] for s in range(2)]
        side = [bank(f"side{h}") for h in range(2)]
        deg_bank = bank("degsum")

        w_loaded = sem("w_loaded")
        xt_loaded = [sem(f"xt_loaded{s}") for s in range(XT_SLOTS)]
        raw_loaded = [sem(f"raw_loaded{s}") for s in range(RAW_SLOTS)]
        nat_loaded = [sem(f"nat_loaded{s}") for s in range(NAT_SLOTS)]
        x_loaded = [sem(f"x_loaded{s}") for s in range(X_SLOTS)]
        stored = [sem(f"stored{s}") for s in range(X_SLOTS)]
        raw_ready = sem("raw_ready")
        ident_zero = sem("ident_zero")
        ident_ready = sem("ident_ready")
        consts = sem("consts")
        xw_done = sem("xw_done")
        xw_copied = sem("xw_copied")
        diag_ready = sem("diag_ready")
        hi_ready = sem("hi_ready")
        lo_ready = sem("lo_ready")
        halves_used = sem("halves_used")
        summed = sem("summed")
        fold_done = sem("fold_done")
        nat_summed = sem("nat_summed")
        deg_summed = sem("deg_summed")
        var_ready = sem("var_ready")
        root_ready = sem("root_ready")
        dinv_ready = sem("dinv_ready")
        yhi_ready = sem("yhi_ready")
        y_ready = sem("y_ready")
        z_copied = sem("z_copied")
        z_added = sem("z_added")
        turned = sem("turned")
        relu_done = sem("relu_done")
        normed = sem("normed")
        step = sem("step")

        DIAG = [tri(k) + k for k in range(B)]
        ROWS = schedule()
        FINISH = [B - 1] + list(range(B - 1))
        LAST = [ROWS[B - 1 + e][1] + ROWS[B - 1 + e][3] - 1 for e in range(B)]

        SUMMED = [tri(k - 1) + max(j, 1) if k else 0 for k in range(B) for j in range(k + 1)]

        def raw_at(n, a=0, size=BLK):
            return raw[:, bass.ds((n % RAW_SLOTS) * BLK + a, size)]

        def split_at(tensor, n, a=0, size=BLK):
            return tensor[:, bass.ds((n % SPLIT_SLOTS) * BLK + a, size)]

        def zt(k):
            return xw[:, k * T:(k + 1) * T, :].rearrange("p t c -> p (t c)").rearrange(
                "p (c r) -> p c r", c=CT)

        def xslot(e):
            s = e % X_SLOTS
            return natx[:, s * T * C:(s + 1) * T * C].rearrange("p (t c) -> p t c", c=C)

        def relu_slot(e):
            return xts[:, e % XT_SLOTS, :, :].rearrange("p c r -> p (c r)").rearrange(
                "p (t c) -> p t c", c=C)

        def sweep(eng, start, stop, body):
            if stop - start >= 3:
                with eng.Fori(start, stop) as n:
                    body(n)
            else:
                for n in range(start, stop):
                    body(n)

        block = ctx.enter_context(nc.Block())

        @block.sync
        def _(sp):
            sp.dma_start(ws[:, :, :], w).then_inc(w_loaded, 16)

            def load_xt(b):
                if b >= XT_SLOTS:
                    sp.wait_ge(xw_done, 2 * (b - XT_SLOTS) + 2)
                sp.dma_start(xts[:, b % XT_SLOTS, :, :], xt[b]).then_inc(xt_loaded[b % XT_SLOTS], 16)

            def load_raw(n):
                if n >= RAW_SLOTS:
                    sp.wait_ge(lo_ready, 2 * (n - RAW_SLOTS) + 2)
                    if 1 <= n - RAW_SLOTS < tri(EARLY):
                        sp.wait_ge(summed, SUMMED[n - RAW_SLOTS])
                sp.dma_start(raw_at(n), at[n]).then_inc(raw_loaded[n % RAW_SLOTS], 16)

            def load_nat(m):
                if m >= NAT_SLOTS:
                    sp.wait_ge(nat_summed, m - NAT_SLOTS + 1)
                s = m % NAT_SLOTS
                sp.dma_start(natx[:, s * BLK:(s + 1) * BLK], nat[m]).then_inc(nat_loaded[s], 16)

            load_xt(0)
            load_xt(1)
            for k in range(B):
                if k < EARLY:
                    for j in range(k + 1):
                        load_raw(tri(k) + j)
                    for i in range(B - 1 - k):
                        load_nat(upper(k) + i)
                        if k == 0 and i + XT_SLOTS < B:
                            load_xt(i + XT_SLOTS)
                else:
                    m = upper(k)
                    for j, turns in enumerate(nat_turns(k)):
                        load_raw(tri(k) + j)
                        for _ in range(turns):
                            load_nat(m)
                            m += 1

            sp.wait_ge(nat_summed, upper(B))

            def load_x(e):
                if e >= X_SLOTS:
                    sp.wait_ge(stored[e % X_SLOTS], 16 * (e // X_SLOTS))
                sp.dma_start(xslot(e), x[FINISH[e]]).then_inc(x_loaded[e % X_SLOTS], 16)

            def store(e):
                sp.wait_ge(normed, T * (e + 1))
                sp.dma_start(out[FINISH[e]], xslot(e)).then_inc(stored[e % X_SLOTS], 16)

            for e in range(X_SLOTS):
                load_x(e)
            n = PHASE1
            for e in range(B):
                stop = min(TOTAL, LAST[e] + RAW_SLOTS + 5)
                for i in range(n, stop):
                    load_raw(i)
                n = max(n, stop)
                store(e)
                if e + X_SLOTS < B:
                    load_x(e + X_SLOTS)
            for s in range(X_SLOTS):
                sp.wait_ge(stored[s], 16 * len(range(s, B, X_SLOTS)))

        @block.gpsimd
        def _(pool):
            nc.gpsimd.memset(ident[:, :], 0.0).then_inc(ident_zero, 1)
            pool.wait_ge(ident_zero, 1)
            nc.gpsimd.affine_select(out=ident[:, :], in_=ident[:, :], compare_op=ALU.not_equal, fill=1.0,
                                    base=0, pattern=[[-1, P]], channel_multiplier=1).then_inc(ident_ready, 1)
            with pool.Fori(0, TOTAL // RAW_SLOTS) as i:
                for s in range(RAW_SLOTS):
                    pool.wait_ge(raw_loaded[s], 16 * (i + 1))
                    pool.sem_inc(raw_ready, 1)

        @block.scalar
        def _(act):
            def round_hi(n):
                act.wait_ge(raw_ready, n + 1)
                for h in range(2):
                    if not isinstance(n, int) or n >= SPLIT_SLOTS:
                        act.wait_ge(halves_used, 2 * (n - SPLIT_SLOTS) + h + 1)
                    nc.scalar.activation(split_at(hi, n, h * HALF, HALF), raw_at(n, h * HALF, HALF),
                                         ACT.Copy).then_inc(hi_ready, 1)

            def round_diag(k):
                act.wait_ge(diag_ready, k + 1)
                round_hi(DIAG[k])

            def sum_nat(k, i):
                m = upper(k) + i
                s = m % NAT_SLOTS
                act.wait_ge(nat_loaded[s], 16 * (m // NAT_SLOTS + 1))
                if m == 0:
                    act.wait_ge(consts, 1)
                for t in range(T):
                    a = natx[:, s * BLK + t * R:s * BLK + (t + 1) * R]
                    last = nc.scalar.activation(a, a, ACT.Copy, accum_out=natsum[:, k, t, i:i + 1])
                last.then_inc(nat_summed, 1)

            def copy_xw(b):
                for h in range(2):
                    act.wait_ge(xw_done, 2 * b + h + 1)
                    nc.scalar.activation(xw[:, b * T + 2 * h:b * T + 2 * h + 2, :], side[h][:, :],
                                         ACT.Copy).then_inc(xw_copied, 1)

            def take_root(i, src):
                act.wait_ge(var_ready, i + 1)
                nc.scalar.activation(root[:, :], src[:, :], ACT.Sqrt).then_inc(root_ready, 1)

            def hi_of_y(k):
                act.wait_ge(dinv_ready, k + 1)
                for t in range(k * T, (k + 1) * T):
                    nc.scalar.activation(y[:, t, 0, :], xw[:, t, :], ACT.Copy,
                                         scale=dinv[:, t:t + 1]).then_inc(yhi_ready, 1)

            def copy_z(k):
                act.wait_ge(halves_used, 2 * DIAG[k] + 2)
                act.wait_ge(y_ready, k + 1)
                for c in range(CT):
                    last = nc.scalar.activation(zt(k)[:, c, :], zbanks[k % 2][c][:, :], ACT.Copy)
                last.then_inc(z_copied, 1)

            def relu(e):
                k = FINISH[e]
                if e >= XT_SLOTS:
                    act.wait_ge(var_ready, B + e - XT_SLOTS + 1)
                for t in range(T):
                    act.wait_ge(turned, T * e + t // 2 * 2 + 2)
                    nc.scalar.activation(relu_slot(e)[:, t, :], side[t // 2][:, t % 2 * C:(t % 2 + 1) * C],
                                         ACT.Relu, scale=dinv[:, k * T + t:k * T + t + 1]).then_inc(relu_done, 1)

            for k in range(B):
                n0 = tri(k)
                if k == 0:
                    for i in range(B):
                        copy_xw(i)
                        if i < B - 1:
                            sum_nat(0, i)
                elif k < EARLY:
                    round_hi(n0)
                    copy_z(k - 1)
                    sweep(act, n0 + 1, n0 + k, round_hi)
                    for i in range(B - 1 - k):
                        sum_nat(k, i)
                else:
                    i = 0
                    for j, turns in enumerate(nat_turns(k)[:k]):
                        if turns or j < 2:
                            round_hi(n0 + j)
                            first = j + 1
                        if j == 1:
                            copy_z(k - 1)
                        for _ in range(turns):
                            sum_nat(k, i)
                            i += 1
                    sweep(act, n0 + first, n0 + k, round_hi)
                take_root(k, deg)
                hi_of_y(k)
                round_diag(k)

            n = PHASE1
            for e in range(B):
                stop = min(TOTAL, LAST[e] + 3)
                if e == 0:
                    round_hi(n)
                    copy_z(B - 1)
                    n += 1
                sweep(act, n, stop, round_hi)
                n = max(n, stop)
                relu(e)
                stop = min(TOTAL, LAST[e] + 4)
                sweep(act, n, stop, round_hi)
                n = max(n, stop)
                take_root(B + e, var)

        @block.vector
        def _(dve):
            chain = [0]

            def link(instruction):
                chain[0] += 1
                instruction.then_inc(step, 1)
                dve.wait_ge(step, chain[0])

            nc.vector.memset(ones[:, :], 1.0)
            nc.vector.memset(natsum[:, :, :, :], 0.0).then_inc(consts, 1)

            def add_identity(k):
                n = DIAG[k]
                dve.wait_ge(raw_ready, n + 1)
                if k == 0:
                    dve.wait_ge(ident_ready, 1)
                s = n % RAW_SLOTS * BLK
                a = raw[:, s:s + T * (R + P)].rearrange("p (u c) -> p u c", u=T)[:, :, 0:P]
                nc.vector.tensor_tensor(a, a, ident[:, :].unsqueeze(1).broadcast_to([P, T, P]),
                                        ALU.add).then_inc(diag_ready, 1)
                dve.wait_ge(diag_ready, k + 1)

            def sum_first(k):
                n0 = tri(k)
                if k == 1:
                    add_identity(k)
                dve.wait_ge(raw_ready, n0 + 2)
                nc.vector.tensor_tensor(colsum[:, :], raw_at(n0), raw_at(n0 + 1), ALU.add).then_inc(summed, 1)

            def sum_next(k):
                def body(n):
                    dve.wait_ge(raw_ready, n + 1)
                    dve.wait_ge(summed, n - k - 1)
                    nc.vector.tensor_tensor(colsum[:, :], colsum[:, :], raw_at(n), ALU.add).then_inc(summed, 1)
                return body

            def fold(k):
                src = raw_at(0) if k == 0 else colsum[:, :]
                if k:
                    dve.wait_ge(summed, tri(k))
                link(nc.vector.tensor_tensor(colsum[:, 0:HALF], src[:, 0:HALF], src[:, HALF:BLK], ALU.add))
                if k:
                    dve.wait_ge(deg_summed, k)
                nc.vector.tensor_tensor(folded[:, :], colsum[:, 0:R], colsum[:, R:2 * R],
                                        ALU.add).then_inc(fold_done, 1)

            def take_half(n, h):
                dve.wait_ge(hi_ready, 2 * n + h + 1)
                nc.vector.tensor_tensor(split_at(lo, n, h * HALF, HALF), raw_at(n, h * HALF, HALF),
                                        split_at(hi_f, n, h * HALF, HALF), ALU.subtract).then_inc(lo_ready, 1)

            def take_lo(n):
                take_half(n, 0)
                take_half(n, 1)

            def refine(d, result):
                link(nc.vector.reciprocal(inv[:, :], root[:, :]))
                link(nc.vector.scalar_tensor_tensor(out=tmp[:, :], in0=inv[:, :], scalar=-0.5, in1=inv[:, :],
                                                    op0=ALU.mult, op1=ALU.mult))
                link(nc.vector.tensor_tensor(tmp[:, :], tmp[:, :], d, ALU.mult))
                return nc.vector.scalar_tensor_tensor(out=result, in0=tmp[:, :], scalar=1.5, in1=inv[:, :],
                                                      op0=ALU.add, op1=ALU.mult)

            def scale_factors(k):
                dve.wait_ge(nat_summed, upper(k + 1))
                link(nc.vector.tensor_reduce(natdeg[:, :], natsum[:, k, :, :], AX.X, ALU.add))
                dve.wait_ge(deg_summed, k + 1)
                nc.vector.tensor_tensor(deg[:, :], deg_bank[:, 0:T], natdeg[:, :], ALU.add).then_inc(var_ready, 1)
                dve.wait_ge(root_ready, k + 1)
                dve.wait_ge(var_ready, k + 1)
                refine(deg[:, :], dinv[:, k * T:(k + 1) * T]).then_inc(dinv_ready, 1)

            def lo_of_y(k):
                dve.wait_ge(dinv_ready, k + 1)
                for t in range(k * T, (k + 1) * T):
                    dve.wait_ge(yhi_ready, t + 1)
                    last = nc.vector.scalar_tensor_tensor(out=y[:, t, 1, :], in0=xw[:, t, :],
                                                          scalar=dinv[:, t:t + 1], in1=y_f[:, t, 0, :],
                                                          op0=ALU.mult, op1=ALU.subtract)
                last.then_inc(y_ready, 1)

            def add_z(e):
                g = B - 1 + e
                a = zt(FINISH[e])
                dve.wait_ge(halves_used, 2 * LAST[e] + 2)
                dve.wait_ge(z_copied, FINISH[e] + 1)
                for c in range(CT):
                    last = nc.vector.tensor_tensor(a[:, c, :], a[:, c, :], zbanks[g % 2][c][:, :], ALU.add)
                last.then_inc(z_added, 1)

            def residual(e, tiles):
                xe = xslot(e)
                dve.wait_ge(x_loaded[e % X_SLOTS], 16 * (e // X_SLOTS + 1))
                for t in tiles:
                    dve.wait_ge(relu_done, T * e + t + 1)
                    link(nc.vector.tensor_tensor(xe[:, t, :], xe[:, t, :], relu_slot(e)[:, t, :], ALU.add))
                    link(nc.vector.bn_stats(stats[:, t, :], xe[:, t, :]))
                    last = nc.vector.bn_aggr(moments[:, t, :], stats[:, t, :])
                if T - 1 in tiles:
                    link(last)
                    nc.vector.tensor_scalar(var[:, :], moments[:, :, 1], EPS, None, ALU.add).then_inc(var_ready, 1)

            def normalise(e):
                xe = xslot(e)
                dve.wait_ge(root_ready, B + e + 1)
                dve.wait_ge(var_ready, B + e + 1)
                link(refine(var[:, :], rstd[:, :]))
                for t in range(T):
                    nc.vector.tensor_scalar(xe[:, t, :], xe[:, t, :], moments[:, t, 0:1], rstd[:, t:t + 1],
                                            ALU.subtract, ALU.mult).then_inc(normed, 1)

            for k in range(B):
                n0 = tri(k)
                if k == 0:
                    add_identity(0)
                    fold(0)
                elif k == 1:
                    take_lo(n0)
                    sum_first(1)
                    fold(1)
                elif k == 2:
                    take_lo(n0)
                    sum_first(2)
                    take_lo(n0 + 1)
                    add_identity(2)
                    sum_next(2)(n0 + 2)
                    fold(2)
                else:
                    sum_first(k)
                    take_lo(n0)
                    sum_next(k)(n0 + 2)

                    def middle(n, following=sum_next(k)):
                        take_lo(n)
                        following(n + 2)

                    sweep(dve, n0 + 1, n0 + k - 2, middle)
                    take_lo(n0 + k - 2)
                    add_identity(k)
                    sum_next(k)(n0 + k)
                    fold(k)
                    take_lo(n0 + k - 1)
                scale_factors(k)
                lo_of_y(k)
                take_lo(n0 + k)

            n = PHASE1
            for e in range(B):
                for after, attend in ((1, add_z), (2, lambda e: residual(e, (0, 1))),
                                      (3, lambda e: residual(e, (2, 3))), (4, normalise)):
                    if e == 0 and after == 1:
                        take_lo(n)
                        n += 1
                        continue
                    stop = min(TOTAL, LAST[e] + after + 1)
                    sweep(dve, n, stop, take_lo)
                    n = max(n, stop)
                    attend(e)

        @block.tensor
        def _(pe):
            def multiply_x(b):
                s = b % XT_SLOTS
                if b == 0:
                    pe.wait_ge(w_loaded, 16)
                pe.wait_ge(xt_loaded[s], 16 * (b // XT_SLOTS + 1))
                for h in range(2):
                    if b:
                        pe.wait_ge(xw_copied, 2 * (b - 1) + h + 1)
                    for q in range(2):
                        t = 2 * h + q
                        for c in range(CT):
                            last = nc.tensor.matmul(side[h][:, q * C:(q + 1) * C],
                                                    xts[:, s, c, t * P:(t + 1) * P], ws[:, c, :],
                                                    start=(c == 0), stop=(c == CT - 1))
                    last.then_inc(xw_done, 1)

            def sum_degrees(k):
                pe.wait_ge(fold_done, k + 1)
                if k == 0:
                    pe.wait_ge(consts, 1)
                else:
                    pe.wait_ge(var_ready, k)
                for t in range(T):
                    last = nc.tensor.matmul(deg_bank[:, t:t + 1], folded[:, t * P:(t + 1) * P], ones[:, :],
                                            start=True, stop=True)
                last.then_inc(deg_summed, 1)

            def multiply(g, n, j, first, last):
                z = zbanks[g % 2]
                if first and 2 <= g < B + 2:
                    pe.wait_ge(z_copied, g - 1)
                elif first and g >= B + 2:
                    pe.wait_ge(z_added, g - B - 1)
                pe.wait_ge(y_ready, j + 1)
                for h in range(2):
                    pe.wait_ge(lo_ready, 2 * n + h + 1)
                    for u in range(h * T // 2, (h + 1) * T // 2):
                        a = n % SPLIT_SLOTS * BLK + u * R
                        opens, closes = first and u == 0, last and u == T - 1
                        for c in range(CT):
                            y_hi = y[:, j * T + u, 0, c * P:(c + 1) * P]
                            y_lo = y[:, j * T + u, 1, c * P:(c + 1) * P]
                            nc.tensor.matmul(z[c][:, :], y_hi, hi[:, a:a + R], start=opens, stop=False)
                            nc.tensor.matmul(z[c][:, :], y_hi, lo[:, a:a + R], start=False, stop=False)
                            done = nc.tensor.matmul(z[c][:, :], y_lo, hi[:, a:a + R], start=False, stop=closes)
                    done.then_inc(halves_used, 1)

            def turn_back(e):
                k = FINISH[e]
                if e:
                    pe.wait_ge(z_added, e)
                    pe.wait_ge(relu_done, T * e)
                else:
                    pe.wait_ge(z_copied, B)
                    pe.wait_ge(xw_copied, 2 * B)
                for t in range(T):
                    for c in range(CT):
                        a = t % 2 * C + c * P
                        last = nc.tensor.transpose(side[t // 2][:, a:a + P], zt(k)[:, c, t * P:(t + 1) * P],
                                                   ident[:, :])
                    last.then_inc(turned, 1)

            for b in range(B):
                multiply_x(b)
            for g, (k, n0, j0, count) in enumerate(ROWS):
                for i in range(count):
                    if g < B and i == (k if k < EARLY else k - 1):
                        sum_degrees(k)
                    multiply(g, n0 + i, j0 + i, i == 0, i == count - 1)
                    for e in range(B):
                        if n0 + i == LAST[e] + 1:
                            turn_back(e)
            turn_back(B - 1)


def kernel(x, adj, L0_gnn_weight):
    import numpy as np
    import concourse.bacc as bacc
    from concourse.bass_utils import run_bass_kernel_spmd

    x, adj, weight = (np.asarray(a) for a in (x, adj, L0_gnn_weight))
    blocks = adj.reshape(B, T, P, B, T, P)
    lower = [(k, j) for k in range(B) for j in range(k + 1)]
    higher = [(k, j) for k in range(B) for j in range(k + 1, B)]
    at = np.stack([blocks[k, :, :, j].transpose(3, 2, 0, 1).reshape(P, BLK) for k, j in lower + higher])
    nat = np.stack([blocks[k, :, :, j].transpose(1, 0, 2, 3).reshape(P, BLK) for k, j in higher])
    xt = np.ascontiguousarray(x.reshape(B, R, 2, P).transpose(0, 3, 2, 1))
    xn = np.ascontiguousarray(x.reshape(B, T, P, C).transpose(0, 2, 1, 3))
    wn = np.ascontiguousarray(weight.reshape(2, P, C).transpose(1, 0, 2))

    nc = bacc.Bacc("TRN2", target_bir_lowering=False, num_devices=1)
    arrays = {"in_at": at, "in_nat": nat, "in_xt": xt, "in_w": wn, "in_x": xn}
    aps = [nc.dram_tensor(name, a.shape, mybir.dt.from_np(a.dtype), kind="ExternalInput").ap()
           for name, a in arrays.items()]
    aps.append(nc.dram_tensor("out", xn.shape, mybir.dt.float32, kind="ExternalOutput").ap())
    build(nc, *aps)
    r = run_bass_kernel_spmd(nc, [arrays], core_ids=[0])
    got = r.results[0]["out"]
    return np.ascontiguousarray(got.transpose(0, 2, 1, 3)).reshape(N, C)
```

```python
import concourse.bass as bass
from concourse import mybir
from contextlib import ExitStack

P = 128
N = 4096
C = 256
CT = C // P
R = 512
T = R // P
B = N // R
BLK = T * R
HALF = BLK // 2
EPS = 1e-5

RAW_SLOTS = 4
SPLIT_SLOTS = 2
NAT_SLOTS = 3
XT_SLOTS = 2
X_SLOTS = 5


def low(k):
    return max(k + 1, 2)


def start(k):
    return sum(low(r) for r in range(k))


COPIED = (5, 4)


def untransposed(k):
    return list(range(low(k), B)) + [j for j in range(low(k)) if (k, j) == COPIED]


def upper(k):
    return sum(len(untransposed(r)) for r in range(k))


STREAM1 = [(0, 0), (1, 0), (2, 0), (0, 1), (1, 1), (2, 1), (3, 0), (2, 2),
           (3, 1), (3, 2), (4, 0), (3, 3), (4, 1), (4, 2), (4, 3), (5, 0),
           (4, 4), (5, 1), (5, 2), (5, 3), (5, 4), (5, 5)]
STREAM1 += [(k, j) for k in range(B) for j in range(low(k)) if (k, j) not in STREAM1]


AHEAD = [3, 7, 11, 16]


def place(k, j):
    return STREAM1.index((k, j))


BY_VECTOR = [1, 3, 5, upper(1) + 1, upper(1) + 3, upper(1) + 5, upper(2) + 4]
PHASE1 = start(B)
TOTAL = B * B
ORDER = [3, 6, 2, 5, 1, 4, 0]


def schedule():
    rows = [(k, [(place(k, j), j) for j in range(low(k))]) for k in range(B)]
    n = PHASE1
    for k in ORDER:
        rows.append((k, [(n + i, low(k) + i) for i in range(B - low(k))]))
        n += B - low(k)
    return rows


def build(nc, at, nat, xt, w, x, out):
    f32 = mybir.dt.float32
    f32r = mybir.dt.float32r
    ALU = mybir.AluOpType
    ACT = mybir.ActivationFunctionType
    AX = mybir.AxisListType

    ctx = ExitStack()
    with ctx:
        def sb(name, shape, dt=f32):
            return ctx.enter_context(nc.sbuf_tensor(name, shape, dt))

        def bank(name):
            return ctx.enter_context(nc.psum_tensor(name, [P, 512], f32))

        def sem(name):
            return ctx.enter_context(nc.semaphore(name))

        raw = sb("raw", [P, RAW_SLOTS * BLK])
        hi = sb("hi", [P, SPLIT_SLOTS * BLK], f32r)
        lo = sb("lo", [P, SPLIT_SLOTS * BLK], f32r)
        hi_f = hi[:, :].bitcast(f32)
        natx = sb("natx", [P, NAT_SLOTS * BLK])
        y = sb("y", [P, N // P, 2, C], f32r)
        y_f = y[:, :, :, :].bitcast(f32)
        xw = sb("xw", [P, N // P, C])
        colsum = sb("colsum", [P, BLK])
        folded = sb("folded", [P, R])
        xts = sb("xts", [P, XT_SLOTS, CT, R])
        ws = sb("ws", [P, CT, C])
        ones = sb("ones", [P, 1])
        ident = sb("ident", [P, P])
        natsum = sb("natsum", [P, B, T, B])
        natdeg = sb("natdeg", [P, T])
        deg = sb("deg", [P, T])
        root = sb("root", [P, 2, T])
        inv = sb("inv", [P, T])
        tmp = sb("tmp", [P, T])
        dinv = sb("dinv", [P, N // P])
        stats = sb("stats", [P, 2, T, 6])
        moments = sb("moments", [P, 2, T, 2])
        var = sb("var", [P, 2, T])
        rstd = sb("rstd", [P, T])

        zmain = [[bank(f"z{s}{c}") for c in range(CT)] for s in range(2)]
        side = [bank(f"side{h}") for h in range(2)]
        deg_bank = bank("degsum")

        w_loaded = sem("w_loaded")
        xt_loaded = [sem(f"xt_loaded{s}") for s in range(XT_SLOTS)]
        raw_loaded = [sem(f"raw_loaded{s}") for s in range(RAW_SLOTS)]
        nat_loaded = [sem(f"nat_loaded{s}") for s in range(NAT_SLOTS)]
        x_loaded = [sem(f"x_loaded{s}") for s in range(X_SLOTS)]
        stored = [sem(f"stored{s}") for s in range(X_SLOTS)]
        raw_ready = sem("raw_ready")
        ident_zero = sem("ident_zero")
        ident_ready = sem("ident_ready")
        consts = sem("consts")
        xw_done = sem("xw_done")
        xw_copied = sem("xw_copied")
        diag_ready = sem("diag_ready")
        hi_ready = sem("hi_ready")
        lo_ready = sem("lo_ready")
        halves_used = sem("halves_used")
        summed = sem("summed")
        fold_done = sem("fold_done")
        nat_summed = sem("nat_summed")
        nat_summed_v = sem("nat_summed_v")
        deg_summed = sem("deg_summed")
        var_ready = sem("var_ready")
        root_ready = sem("root_ready")
        dinv_ready = sem("dinv_ready")
        yhi_ready = sem("yhi_ready")
        y_ready = sem("y_ready")
        z_copied = sem("z_copied")
        z_added = sem("z_added")
        turned = sem("turned")
        relu_done = sem("relu_done")
        normed = sem("normed")
        step = sem("step")

        DIAG = [place(k, k) for k in range(B)]
        FIRST_USE = [min(place(k, j) for k in range(B) if (k, j) in STREAM1) for j in range(B)]
        ROWS = schedule()
        FINISH = [B - 1] + ORDER
        HALVES = [(0, T // 2), (T // 2, T)]
        LAST = [ROWS[B - 1 + e][1][-1][0] for e in range(B)]

        SUMMED, steps = {}, 0
        for k in range(B):
            for j in range(low(k)):
                steps += j != 1 and (k, j) != COPIED
                SUMMED[place(k, j)] = steps

        def raw_at(n, a=0, size=BLK):
            return raw[:, bass.ds((n % RAW_SLOTS) * BLK + a, size)]

        def split_at(tensor, n, a=0, size=BLK):
            return tensor[:, bass.ds((n % SPLIT_SLOTS) * BLK + a, size)]

        def zbanks(g):
            return side if g == 2 else zmain[g % 2]

        def zt(k):
            return xw[:, k * T:(k + 1) * T, :].rearrange("p t c -> p (t c)").rearrange(
                "p (c r) -> p c r", c=CT)

        def xslot(e):
            s = e % X_SLOTS
            return natx[:, s * T * C:(s + 1) * T * C].rearrange("p (t c) -> p t c", c=C)

        def relu_slot(e):
            return xts[:, e % XT_SLOTS, :, :].rearrange("p c r -> p (c r)").rearrange(
                "p (t c) -> p t c", c=C)

        def sweep(eng, start, stop, body):
            if stop - start >= 3:
                with eng.Fori(start, stop) as n:
                    body(n)
            else:
                for n in range(start, stop):
                    body(n)

        block = ctx.enter_context(nc.Block())

        @block.sync
        def _(sp):
            sp.dma_start(ws[:, :, :], w).then_inc(w_loaded, 16)

            def load_xt(b):
                if b >= XT_SLOTS:
                    sp.wait_ge(xw_done, 2 * (b - XT_SLOTS) + 2)
                sp.dma_start(xts[:, b % XT_SLOTS, :, :], xt[b]).then_inc(xt_loaded[b % XT_SLOTS], 16)

            def load_raw(n):
                if n >= RAW_SLOTS:
                    sp.wait_ge(lo_ready, 2 * (n - RAW_SLOTS) + 2)
                    if n - RAW_SLOTS < start(6):
                        sp.wait_ge(summed, SUMMED[n - RAW_SLOTS])
                sp.dma_start(raw_at(n), at[n]).then_inc(raw_loaded[n % RAW_SLOTS], 16)

            def load_nat(m):
                if m >= NAT_SLOTS:
                    former = m - NAT_SLOTS
                    vector = sum(v <= former for v in BY_VECTOR)
                    if former in BY_VECTOR:
                        sp.wait_ge(nat_summed_v, vector)
                    else:
                        sp.wait_ge(nat_summed, former - vector + 1)
                s = m % NAT_SLOTS
                sp.dma_start(natx[:, s * BLK:(s + 1) * BLK], nat[m]).then_inc(nat_loaded[s], 16)

            def load_nats(k, first, stop):
                for i in range(first, stop):
                    load_nat(upper(k) + i)

            load_xt(0)
            load_xt(1)
            load_raw(0)
            load_raw(3)
            for i in range(B - low(0)):
                load_nat(i)
                if i + 2 < B - 2:
                    load_xt(i + 2)
            load_raw(1)
            load_xt(6)
            load_raw(2)
            load_xt(7)
            load_raw(4)
            load_nats(1, 0, 6)
            load_raw(5)
            load_nats(2, 0, 3)
            load_raw(7)
            load_raw(6)
            load_nats(2, 3, 5)
            load_raw(8)
            load_nats(3, 0, 1)
            load_raw(9)
            load_nats(3, 1, 2)
            load_raw(11)
            load_nats(3, 2, 3)
            load_raw(10)
            load_nats(3, 3, 4)
            load_raw(12)
            load_nats(4, 0, 1)
            load_raw(13)
            load_nats(4, 1, 2)
            load_raw(14)
            load_nats(4, 2, 3)
            load_raw(16)
            load_raw(15)
            load_nats(5, 0, 1)
            load_raw(17)
            load_nats(5, 1, 2)
            load_raw(18)
            load_nats(5, 2, 3)
            for n in range(19, 22):
                load_raw(n)
            for k in range(6, B):
                load_raw(start(k))
                load_nats(k, 0, B - low(k))
                for n in range(start(k) + 1, start(k + 1)):
                    load_raw(n)

            sp.wait_ge(nat_summed, upper(B) - len(BY_VECTOR))

            def load_x(e):
                if e >= X_SLOTS:
                    sp.wait_ge(stored[e % X_SLOTS], 16 * (e // X_SLOTS))
                sp.dma_start(xslot(e), x[FINISH[e]]).then_inc(x_loaded[e % X_SLOTS], 16)

            def store(e):
                for a, b in [(0, T)] if e < B - 1 else HALVES:
                    sp.wait_ge(normed, T * e + b)
                    sp.dma_start(out[FINISH[e]][:, a:b, :], xslot(e)[:, a:b, :]).then_inc(stored[e % X_SLOTS], 16)

            for e in range(X_SLOTS):
                load_x(e)
            n = PHASE1
            for e in range(B):
                stop = min(TOTAL, LAST[e] + RAW_SLOTS + 5)
                for i in range(n, stop):
                    load_raw(i)
                n = max(n, stop)
                store(e)
                if e + X_SLOTS < B:
                    load_x(e + X_SLOTS)
            for s in range(X_SLOTS):
                sp.wait_ge(stored[s], 16 * (len(range(s, B, X_SLOTS)) + (s == (B - 1) % X_SLOTS)))

        @block.gpsimd
        def _(pool):
            nc.gpsimd.memset(ident[:, :], 0.0).then_inc(ident_zero, 1)
            pool.wait_ge(ident_zero, 1)
            nc.gpsimd.affine_select(out=ident[:, :], in_=ident[:, :], compare_op=ALU.not_equal, fill=1.0,
                                    base=0, pattern=[[-1, P]], channel_multiplier=1).then_inc(ident_ready, 1)
            with pool.Fori(0, TOTAL // RAW_SLOTS) as i:
                for s in range(RAW_SLOTS):
                    pool.wait_ge(raw_loaded[s], 16 * (i + 1))
                    pool.sem_inc(raw_ready, 1)

        @block.scalar
        def _(act):
            def round_half(n, h):
                if not isinstance(n, int) or n >= SPLIT_SLOTS:
                    act.wait_ge(halves_used, 2 * (n - SPLIT_SLOTS) + h + 1)
                nc.scalar.activation(split_at(hi, n, h * HALF, HALF), raw_at(n, h * HALF, HALF),
                                     ACT.Copy).then_inc(hi_ready, 1)

            def round_hi(n):
                act.wait_ge(raw_ready, n + 1)
                round_half(n, 0)
                round_half(n, 1)

            def round_diag(k):
                act.wait_ge(diag_ready, k + 1)
                round_hi(DIAG[k])

            def sum_nat(k, i):
                m = upper(k) + i
                s = m % NAT_SLOTS
                act.wait_ge(nat_loaded[s], 16 * (m // NAT_SLOTS + 1))
                if m == 0:
                    act.wait_ge(consts, 1)
                for t in range(T):
                    a = natx[:, s * BLK + t * R:s * BLK + (t + 1) * R]
                    last = nc.scalar.activation(a, a, ACT.Copy, accum_out=natsum[:, k, t, i:i + 1])
                last.then_inc(nat_summed, 1)

            def copy_xw(b):
                for h in range(2):
                    act.wait_ge(xw_done, 2 * b + h + 1)
                    nc.scalar.activation(xw[:, b * T + 2 * h:b * T + 2 * h + 2, :], side[h][:, :],
                                         ACT.Copy).then_inc(xw_copied, 1)

            def take_root(i, src, a=0, b=T):
                act.wait_ge(var_ready, i + 1)
                nc.scalar.activation(root[:, i % 2, a:b], src[:, a:b], ACT.Sqrt).then_inc(root_ready, 1)

            def hi_of_y(k):
                act.wait_ge(dinv_ready, k + 1)
                for t in range(k * T, (k + 1) * T):
                    nc.scalar.activation(y[:, t, 0, :], xw[:, t, :], ACT.Copy,
                                         scale=dinv[:, t:t + 1]).then_inc(yhi_ready, 1)

            def round_y(k):
                take_root(k, deg[:, :])
                hi_of_y(k)

            def copy_z(k):
                act.wait_ge(halves_used, 2 * place(k, low(k) - 1) + 2)
                act.wait_ge(y_ready, T * (k + 1))
                for c in range(CT):
                    last = nc.scalar.activation(zt(k)[:, c, :], zbanks(k)[c][:, :], ACT.Copy)
                last.then_inc(z_copied, 1)

            def relu(e, a=0, b=T):
                k = FINISH[e]
                if e >= XT_SLOTS:
                    act.wait_ge(var_ready, B + e - XT_SLOTS + 1)
                for t in range(a, b):
                    act.wait_ge(turned, T * e + t // 2 * 2 + 2)
                    nc.scalar.activation(relu_slot(e)[:, t, :], side[t // 2][:, t % 2 * C:(t % 2 + 1) * C],
                                         ACT.Relu, scale=dinv[:, k * T + t:k * T + t + 1]).then_inc(relu_done, 1)

            act.wait_ge(consts, 1)
            nc.scalar.activation(root[:, 0, 0:1], ones[:, :], ACT.Sqrt)

            copy_xw(0)
            copy_xw(1)
            sum_nat(0, 0)
            copy_xw(2)
            round_diag(0)
            copy_xw(3)
            sum_nat(0, 2)
            copy_xw(4)
            sum_nat(0, 4)
            copy_xw(5)
            round_y(0)

            round_hi(1)
            sum_nat(1, 0)
            copy_xw(6)
            round_hi(2)
            sum_nat(1, 2)
            copy_xw(7)
            sum_nat(1, 4)
            round_hi(3)
            round_y(1)
            round_diag(1)

            sum_nat(2, 0)
            sum_nat(2, 1)
            sum_nat(2, 2)
            round_hi(5)
            copy_z(0)
            round_hi(6)
            copy_z(1)
            sum_nat(2, 3)
            round_diag(2)
            round_y(2)

            sum_nat(3, 0)
            round_hi(8)
            sum_nat(3, 1)
            round_hi(9)
            copy_z(2)
            sum_nat(3, 2)
            round_hi(10)
            sum_nat(3, 3)
            take_root(3, deg[:, :])
            act.wait_ge(diag_ready, 4)
            round_half(11, 0)
            hi_of_y(3)
            round_half(11, 1)

            sum_nat(4, 0)
            round_hi(12)
            round_hi(13)
            copy_z(3)
            sum_nat(4, 1)
            round_hi(14)
            sum_nat(4, 2)
            round_hi(15)
            round_diag(4)
            round_y(4)

            sum_nat(5, 0)
            round_hi(17)
            round_hi(18)
            copy_z(4)
            sum_nat(5, 1)
            round_hi(19)
            sum_nat(5, 2)
            round_hi(20)
            round_diag(5)
            round_y(5)

            for k in range(6, B):
                n0 = start(k)
                round_hi(n0)
                round_hi(n0 + 1)
                copy_z(k - 1)
                if B - low(k):
                    sum_nat(k, 0)
                sweep(act, n0 + 2, n0 + k, round_hi)
                round_diag(k)
                round_y(k)

            n = PHASE1
            for busy in sorted({PHASE1, *(n + 2 for n in LAST[:-1]), *(n + 4 for n in LAST[:-1])}):
                sweep(act, n, busy + 1, round_hi)
                n = busy + 1
                if busy == PHASE1:
                    copy_z(B - 1)
                for e in range(B - 1):
                    if busy == LAST[e] + 4:
                        take_root(B + e, var[:, e % 2, :])
                    if busy == LAST[e] + 2:
                        relu(e)
            sweep(act, n, TOTAL, round_hi)
            for h, (a, b) in enumerate(HALVES):
                relu(B - 1, a, b)
                take_root(2 * B - 1 + h, var[:, (B - 1) % 2, :], a, b)

        @block.vector
        def _(dve):
            chain = [0]

            def link(instruction):
                chain[0] += 1
                instruction.then_inc(step, 1)
                dve.wait_ge(step, chain[0])

            nc.vector.memset(ones[:, :], 1.0)
            nc.vector.memset(natsum[:, :, :, :], 0.0).then_inc(consts, 1)

            def wait_block(n):
                if isinstance(n, int) and n in AHEAD:
                    dve.wait_ge(raw_loaded[n % RAW_SLOTS], 16 * (n // RAW_SLOTS + 1))
                else:
                    dve.wait_ge(raw_ready, n + 1)

            def add_identity(k):
                n = DIAG[k]
                wait_block(n)
                if k == 0:
                    dve.wait_ge(ident_ready, 1)
                s = n % RAW_SLOTS * BLK
                a = raw[:, s:s + (T - 1) * (R + P)].rearrange("p (u c) -> p u c", u=T - 1)[:, :, 0:P]
                b = raw[:, s + (T - 1) * (R + P):s + BLK]
                nc.vector.tensor_tensor(a, a, ident[:, :].unsqueeze(1).broadcast_to([P, T - 1, P]), ALU.add)
                nc.vector.tensor_tensor(b, b, ident[:, :], ALU.add).then_inc(diag_ready, 1)
                dve.wait_ge(diag_ready, k + 1)

            def sum_first(k):
                if k < 2:
                    add_identity(k)
                if k:
                    dve.wait_ge(fold_done, k)
                wait_block(place(k, 1))
                nc.vector.tensor_tensor(colsum[:, :], raw_at(place(k, 0)), raw_at(place(k, 1)),
                                        ALU.add).then_inc(summed, 1)

            def sum_next(n, former):
                wait_block(n)
                dve.wait_ge(summed, former)
                nc.vector.tensor_tensor(colsum[:, :], colsum[:, :], raw_at(n), ALU.add).then_inc(summed, 1)

            def sum_nat(k, i):
                m = upper(k) + i
                s = m % NAT_SLOTS
                dve.wait_ge(nat_loaded[s], 16 * (m // NAT_SLOTS + 1))
                nc.vector.tensor_reduce(natsum[:, k, :, i],
                                        natx[:, s * BLK:(s + 1) * BLK].rearrange("p (t r) -> p t r", t=T),
                                        AX.X, ALU.add).then_inc(nat_summed_v, 1)

            def fold(k):
                dve.wait_ge(summed, SUMMED[place(k, low(k) - 1)])
                link(nc.vector.tensor_tensor(colsum[:, 0:HALF], colsum[:, 0:HALF], colsum[:, HALF:BLK], ALU.add))
                if k:
                    dve.wait_ge(deg_summed, k)
                nc.vector.tensor_tensor(folded[:, :], colsum[:, 0:R], colsum[:, R:2 * R],
                                        ALU.add).then_inc(fold_done, 1)

            def take_half(n, h):
                dve.wait_ge(hi_ready, 2 * n + h + 1)
                nc.vector.tensor_tensor(split_at(lo, n, h * HALF, HALF), raw_at(n, h * HALF, HALF),
                                        split_at(hi_f, n, h * HALF, HALF), ALU.subtract).then_inc(lo_ready, 1)

            def take_lo(n):
                take_half(n, 0)
                take_half(n, 1)

            def refine(i, d, result, a=0, b=T):
                dve.wait_ge(root_ready, i + 1)
                dve.wait_ge(var_ready, i + 1)
                link(nc.vector.reciprocal(inv[:, a:b], root[:, i % 2, a:b]))
                link(nc.vector.scalar_tensor_tensor(out=tmp[:, a:b], in0=inv[:, a:b], scalar=-0.5, in1=inv[:, a:b],
                                                    op0=ALU.mult, op1=ALU.mult))
                link(nc.vector.tensor_tensor(tmp[:, a:b], tmp[:, a:b], d[:, a:b], ALU.mult))
                return nc.vector.scalar_tensor_tensor(out=result[:, a:b], in0=tmp[:, a:b], scalar=1.5,
                                                      in1=inv[:, a:b], op0=ALU.add, op1=ALU.mult)

            def scale_factors(k):
                dve.wait_ge(nat_summed, upper(k + 1) - sum(v < upper(k + 1) for v in BY_VECTOR))
                if any(upper(k) <= v < upper(k + 1) for v in BY_VECTOR):
                    dve.wait_ge(nat_summed_v, sum(v < upper(k + 1) for v in BY_VECTOR))
                link(nc.vector.tensor_reduce(natdeg[:, :], natsum[:, k, :, :], AX.X, ALU.add))
                dve.wait_ge(deg_summed, k + 1)
                nc.vector.tensor_tensor(deg[:, :], deg_bank[:, 0:T], natdeg[:, :], ALU.add).then_inc(var_ready, 1)
                refine(k, deg, dinv[:, k * T:(k + 1) * T]).then_inc(dinv_ready, 1)

            def lo_of_y(k):
                dve.wait_ge(dinv_ready, k + 1)
                for t in range(k * T, (k + 1) * T):
                    dve.wait_ge(yhi_ready, t + 1)
                    nc.vector.scalar_tensor_tensor(out=y[:, t, 1, :], in0=xw[:, t, :],
                                                   scalar=dinv[:, t:t + 1], in1=y_f[:, t, 0, :],
                                                   op0=ALU.mult, op1=ALU.subtract).then_inc(y_ready, 1)

            def add_z(e, g, n, a=0, b=T):
                z = zt(FINISH[e])
                dve.wait_ge(halves_used, 2 * n + 2)
                dve.wait_ge(z_copied, FINISH[e] + 1)
                for c in range(CT):
                    last = nc.vector.tensor_tensor(z[:, c, a * P:b * P], z[:, c, a * P:b * P],
                                                   zbanks(g)[c][:, a * P:b * P], ALU.add)
                last.then_inc(z_added, 1)

            def residual(e, tiles):
                xe = xslot(e)
                dve.wait_ge(x_loaded[e % X_SLOTS], 16 * (e // X_SLOTS + 1))
                for t in tiles:
                    dve.wait_ge(relu_done, T * e + t + 1)
                    last = nc.vector.tensor_tensor(xe[:, t, :], xe[:, t, :], relu_slot(e)[:, t, :], ALU.add)
                link(last)
                for t in tiles:
                    last = nc.vector.bn_stats(stats[:, e % 2, t, :], xe[:, t, :])
                link(last)
                for t in tiles:
                    last = nc.vector.bn_aggr(moments[:, e % 2, t, :], stats[:, e % 2, t, :])
                link(last)

            def variance(e, a=0, b=T):
                nc.vector.tensor_scalar(var[:, e % 2, a:b], moments[:, e % 2, a:b, 1], EPS, None,
                                        ALU.add).then_inc(var_ready, 1)

            def normalise(e, i, a=0, b=T):
                xe = xslot(e)
                link(refine(i, var[:, e % 2, :], rstd, a, b))
                for t in range(a, b):
                    nc.vector.tensor_scalar(xe[:, t, :], xe[:, t, :], moments[:, e % 2, t, 0:1], rstd[:, t:t + 1],
                                            ALU.subtract, ALU.mult).then_inc(normed, 1)

            sum_first(0)
            fold(0)
            sum_nat(0, 1)
            take_lo(0)
            sum_nat(0, 3)
            sum_nat(0, 5)
            scale_factors(0)
            lo_of_y(0)

            take_lo(1)
            sum_first(1)
            fold(1)
            sum_nat(1, 1)
            take_lo(2)
            sum_nat(1, 3)
            sum_nat(1, 5)
            scale_factors(1)
            take_half(3, 0)
            lo_of_y(1)
            take_half(3, 1)
            sum_first(2)
            take_lo(4)

            add_identity(2)
            sum_next(7, SUMMED[7] - 1)
            take_lo(5)
            fold(2)
            take_lo(6)
            sum_nat(2, 4)
            scale_factors(2)
            take_half(7, 0)
            lo_of_y(2)
            take_half(7, 1)
            sum_first(3)

            take_lo(8)
            sum_next(9, SUMMED[9] - 1)
            take_lo(9)
            add_identity(3)
            sum_next(11, SUMMED[11] - 1)
            fold(3)
            take_lo(10)
            scale_factors(3)
            take_half(11, 0)
            lo_of_y(3)
            take_half(11, 1)

            sum_first(4)
            take_lo(12)
            take_lo(13)
            sum_next(13, SUMMED[13] - 1)
            sum_next(14, SUMMED[14] - 1)
            take_lo(14)
            add_identity(4)
            sum_next(16, SUMMED[16] - 1)
            fold(4)
            take_lo(15)
            scale_factors(4)
            take_half(16, 0)
            lo_of_y(4)
            take_half(16, 1)

            sum_first(5)
            take_lo(17)
            sum_next(18, SUMMED[18] - 1)
            take_lo(18)
            sum_next(19, SUMMED[19] - 1)
            take_lo(19)
            add_identity(5)
            sum_next(21, SUMMED[21] - 1)
            fold(5)
            take_lo(20)
            scale_factors(5)
            take_half(21, 0)
            lo_of_y(5)
            take_half(21, 1)

            for k in range(6, B):
                n0 = start(k)
                sum_first(k)
                take_lo(n0)
                lag = n0 + 3 - SUMMED[n0 + 2]
                sum_next(n0 + 2, n0 + 2 - lag)

                def middle(n, lag=lag):
                    take_lo(n)
                    sum_next(n + 2, n + 2 - lag)

                sweep(dve, n0 + 1, n0 + k - 2, middle)
                take_lo(n0 + k - 2)
                add_identity(k)
                sum_next(n0 + k, n0 + k - lag)
                fold(k)
                take_lo(n0 + k - 1)
                scale_factors(k)
                take_half(n0 + k, 0)
                lo_of_y(k)
                take_half(n0 + k, 1)

            n = PHASE1
            for busy in sorted({n + after for n in LAST[:-1] for after in (1, 2, 3, 4)}):
                sweep(dve, n, busy + 1, take_lo)
                n = busy + 1
                for e in range(1, B - 1):
                    if busy == LAST[e] + 1:
                        add_z(e, B - 1 + e, LAST[e])
                for e in range(B - 1):
                    if busy == LAST[e] + 2:
                        residual(e, (0, 1))
                    elif busy == LAST[e] + 3:
                        residual(e, (2, 3))
                        variance(e)
                    elif busy == LAST[e] + 4:
                        normalise(e, B + e)
            sweep(dve, n, TOTAL, take_lo)
            add_z(B - 1, 2 * B - 2, TOTAL - 3)
            dve.wait_ge(z_added, B - 1)
            add_z(B - 1, 2 * B - 1, TOTAL - 2, *HALVES[0])
            residual(B - 1, range(*HALVES[0]))
            variance(B - 1, *HALVES[0])
            add_z(B - 1, 2 * B, TOTAL - 1, *HALVES[1])
            normalise(B - 1, 2 * B - 1, *HALVES[0])
            residual(B - 1, range(*HALVES[1]))
            variance(B - 1, *HALVES[1])
            normalise(B - 1, 2 * B, *HALVES[1])

        @block.tensor
        def _(pe):
            def multiply_x(b):
                s = b % XT_SLOTS
                if b == 0:
                    pe.wait_ge(w_loaded, 16)
                pe.wait_ge(xt_loaded[s], 16 * (b // XT_SLOTS + 1))
                for h in range(2):
                    if b:
                        pe.wait_ge(xw_copied, 2 * (b - 1) + h + 1)
                    for q in range(2):
                        t = 2 * h + q
                        for c in range(CT):
                            last = nc.tensor.matmul(side[h][:, q * C:(q + 1) * C],
                                                    xts[:, s, c, t * P:(t + 1) * P], ws[:, c, :],
                                                    start=(c == 0), stop=(c == CT - 1))
                    last.then_inc(xw_done, 1)

            def sum_degrees(k):
                pe.wait_ge(fold_done, k + 1)
                if k == 0:
                    pe.wait_ge(consts, 1)
                else:
                    pe.wait_ge(var_ready, k)
                for t in range(T):
                    last = nc.tensor.matmul(deg_bank[:, t:t + 1], folded[:, t * P:(t + 1) * P], ones[:, :],
                                            start=True, stop=True)
                last.then_inc(deg_summed, 1)

            def multiply(g, n, j, first, last):
                z = zbanks(g)
                if first and g == 2:
                    pe.wait_ge(xw_copied, 2 * B)
                elif first and 3 <= g < B + 2:
                    pe.wait_ge(z_copied, g - 1)
                elif first and g >= B + 2:
                    pe.wait_ge(z_added, g - B - 1)
                for h in range(2):
                    pe.wait_ge(lo_ready, 2 * n + h + 1)
                    for u in range(h * T // 2, (h + 1) * T // 2):
                        if n == FIRST_USE[j]:
                            pe.wait_ge(y_ready, T * j + u + 1)
                        a = n % SPLIT_SLOTS * BLK + u * R
                        opens, closes = first and u == 0, last and u == T - 1
                        for c in range(CT):
                            y_hi = y[:, j * T + u, 0, c * P:(c + 1) * P]
                            y_lo = y[:, j * T + u, 1, c * P:(c + 1) * P]
                            nc.tensor.matmul(z[c][:, :], y_hi, hi[:, a:a + R], start=opens, stop=False)
                            nc.tensor.matmul(z[c][:, :], y_hi, lo[:, a:a + R], start=False, stop=False)
                            done = nc.tensor.matmul(z[c][:, :], y_lo, hi[:, a:a + R], start=False, stop=closes)
                    done.then_inc(halves_used, 1)

            def multiply_last():
                _, blocks = ROWS[-1]
                for r, (a, b) in enumerate(HALVES):
                    z = zbanks(2 * B - 1 + r)
                    pe.wait_ge(z_added, B - 2 + r)
                    for n, j in blocks[-2:]:
                        for u in range(T):
                            if r == 0:
                                pe.wait_ge(lo_ready, 2 * n + u // (T // 2) + 1)
                            if r == 1 and n == TOTAL - 2 and u == T // 2:
                                turn_back(B - 1, 0, T // 2)
                            at = n % SPLIT_SLOTS * BLK + u * R
                            opens = n == TOTAL - 2 and u == 0
                            closes = n == TOTAL - 1 and u == T - 1
                            for c in range(CT):
                                y_hi = y[:, j * T + u, 0, c * P:(c + 1) * P]
                                y_lo = y[:, j * T + u, 1, c * P:(c + 1) * P]
                                zr = z[c][:, a * P:b * P]
                                h, l = hi[:, at + a * P:at + b * P], lo[:, at + a * P:at + b * P]
                                nc.tensor.matmul(zr, y_hi, h, start=opens, stop=False)
                                nc.tensor.matmul(zr, y_hi, l, start=False, stop=False)
                                done = nc.tensor.matmul(zr, y_lo, h, start=False, stop=closes)
                    done.then_inc(halves_used, 2)

            def turn_back(e, a=0, b=T):
                k = FINISH[e]
                if e:
                    pe.wait_ge(z_added, e if e < B - 1 else B - 1 + b // (T // 2))
                    pe.wait_ge(relu_done, T * e)
                else:
                    pe.wait_ge(z_copied, B)
                    pe.wait_ge(xw_copied, 2 * B)
                for t in range(a, b):
                    for c in range(CT):
                        s = t % 2 * C + c * P
                        last = nc.tensor.transpose(side[t // 2][:, s:s + P], zt(k)[:, c, t * P:(t + 1) * P],
                                                   ident[:, :])
                    last.then_inc(turned, 1)

            for b in range(B - 2):
                multiply_x(b)
            for n, (k, j) in enumerate(STREAM1):
                if n == 0:
                    sum_degrees(0)
                for row in range(1, B):
                    if n == DIAG[row] - 1:
                        sum_degrees(row)
                multiply(k, n, j, j == 0, j == low(k) - 1)
                if n == 0:
                    multiply_x(B - 2)
                    multiply_x(B - 1)
            for g in range(B, len(ROWS)):
                k, blocks = ROWS[g]
                for n, j in blocks:
                    if n < TOTAL - 2:
                        multiply(g, n, j, (n, j) == blocks[0], (n, j) == blocks[-1] or n == TOTAL - 3)
                    for e in range(B - 1):
                        if n == LAST[e] + 1:
                            turn_back(e)
            multiply_last()
            turn_back(B - 1, T // 2, T)


def kernel(x, adj, L0_gnn_weight):
    import numpy as np
    import concourse.bacc as bacc
    from concourse.bass_utils import run_bass_kernel_spmd

    x, adj, weight = (np.asarray(a) for a in (x, adj, L0_gnn_weight))
    tiles = adj.reshape(B, T, P, B, T, P)
    numbered = sorted((n, k, j) for k, blocks in schedule() for n, j in blocks)
    stream = [(k, j) for _, k, j in numbered]
    summed_only = [(k, j) for k in range(B) for j in untransposed(k)]
    at = np.stack([tiles[k, :, :, j].transpose(3, 2, 0, 1).reshape(P, BLK) for k, j in stream])
    nat = np.stack([tiles[k, :, :, j].transpose(1, 0, 2, 3).reshape(P, BLK) for k, j in summed_only])
    xt = np.ascontiguousarray(x.reshape(B, R, 2, P).transpose(0, 3, 2, 1))
    xn = np.ascontiguousarray(x.reshape(B, T, P, C).transpose(0, 2, 1, 3))
    wn = np.ascontiguousarray(weight.reshape(2, P, C).transpose(1, 0, 2))

    nc = bacc.Bacc("TRN2", target_bir_lowering=False, num_devices=1)
    arrays = {"in_at": at, "in_nat": nat, "in_xt": xt, "in_w": wn, "in_x": xn}
    aps = [nc.dram_tensor(name, a.shape, mybir.dt.from_np(a.dtype), kind="ExternalInput").ap()
           for name, a in arrays.items()]
    aps.append(nc.dram_tensor("out", xn.shape, mybir.dt.float32, kind="ExternalOutput").ap())
    build(nc, *aps)
    r = run_bass_kernel_spmd(nc, [arrays], core_ids=[0])
    got = r.results[0]["out"]
    return np.ascontiguousarray(got.transpose(0, 2, 1, 3)).reshape(N, C)
```
